# Optimizing a Trainium2 kernel written in Bass

```python
import numpy as np
import jax
import jax.numpy as jnp

def _softmax(x, axis=-1):
    return jax.nn.softmax(x, axis=axis)

def _gelu(x):
    return jax.nn.gelu(x, approximate=True)

def _silu(x):
    return jax.nn.silu(x)

def _sigmoid(x):
    return jax.nn.sigmoid(x)

def _layernorm(x, axis=-1, eps=1e-05):
    m = jnp.mean(x, axis=axis, keepdims=True)
    v = jnp.var(x, axis=axis, keepdims=True)
    return (x - m) / jnp.sqrt(v + eps)

def _scatter_add(tgt, idx, src, axis=0):
    return tgt.at[idx].add(src)

def _segment_sum(src, seg, n):
    return jax.ops.segment_sum(src, seg, n)
kernel_name = 'mk_seq_postln_d1_jaxref_r4_756a73'

def setup_inputs(seed: int=0):
    np.random.seed(seed)
    _w = jnp.asarray

    def _L0_attn_setup():
        import jax, jax.numpy as jnp
        from jax import lax
        import numpy as np
        DIM = 256
        HEADS = 16
        B, N = (2, 512)

        def sn_dense(x, W, u, sigma_param):
            v = lax.stop_gradient(W @ u)
            v = lax.stop_gradient(v / jnp.linalg.norm(v, ord=2))
            u2 = lax.stop_gradient(W.T @ v)
            u2 = lax.stop_gradient(u2 / jnp.linalg.norm(u2, ord=2))
            sigma = jnp.einsum('c,cd,d->', v, W, u2)
            return x @ (sigma_param[0] / sigma * W)
        key = jax.random.key(seed)
        ks = jax.random.split(key, 5)
        std = 0.1
        batch = jax.random.normal(ks[0], (B, N, DIM), dtype=jnp.float32)
        W_qkv = jax.random.normal(ks[1], (DIM, 3 * DIM), dtype=jnp.float32) * std
        W_proj = jax.random.normal(ks[2], (DIM, DIM), dtype=jnp.float32) * std
        u_qkv = jax.random.normal(ks[3], (3 * DIM,), dtype=jnp.float32)
        u_qkv = u_qkv / jnp.linalg.norm(u_qkv)
        u_proj = jax.random.normal(ks[4], (DIM,), dtype=jnp.float32)
        u_proj = u_proj / jnp.linalg.norm(u_proj)
        sigma_qkv = jnp.ones((1,), dtype=jnp.float32)
        sigma_proj = jnp.ones((1,), dtype=jnp.float32)
        return {'batch': batch, 'W_qkv': W_qkv, 'u_qkv': u_qkv, 'sigma_qkv': sigma_qkv, 'W_proj': W_proj, 'u_proj': u_proj, 'sigma_proj': sigma_proj}
    _L0_attn_in = _L0_attn_setup()

    def _L0_ffn_setup():
        import jax, jax.numpy as jnp
        import numpy as np
        FP8_MAX = 448.0
        key = jax.random.key(seed)
        k_x, k_w, k_b = jax.random.split(key, 3)
        B, S, IN, OUT = (4, 2048, 256, 256)
        x = jax.random.normal(k_x, (B, S, IN), dtype=jnp.float32)
        w_fp32 = jax.random.normal(k_w, (OUT, IN), dtype=jnp.float32)
        weight_fp8 = w_fp32.astype(jnp.float8_e4m3fn).astype(jnp.float32)
        bias = jax.random.normal(k_b, (OUT,), dtype=jnp.float32)
        input_scale = jnp.ones((1,), dtype=jnp.float32)
        weight_scale = jnp.ones((1,), dtype=jnp.float32)
        return {'x': x, 'weight_fp8': weight_fp8, 'bias': bias, 'input_scale': input_scale, 'weight_scale': weight_scale}
    _L0_ffn_in = _L0_ffn_setup()
    _d = {'L0_attn_batch': _L0_attn_in['batch'], 'L0_attn_W_qkv': _L0_attn_in['W_qkv'], 'L0_attn_u_qkv': _L0_attn_in['u_qkv'], 'L0_attn_sigma_qkv': _L0_attn_in['sigma_qkv'], 'L0_attn_W_proj': _L0_attn_in['W_proj'], 'L0_attn_u_proj': _L0_attn_in['u_proj'], 'L0_attn_sigma_proj': _L0_attn_in['sigma_proj'], 'L0_ffn_weight_fp8': _L0_ffn_in['weight_fp8'], 'L0_ffn_bias': _L0_ffn_in['bias'], 'L0_ffn_input_scale': _L0_ffn_in['input_scale'], 'L0_ffn_weight_scale': _L0_ffn_in['weight_scale']}
    _x0 = _d['L0_attn_batch']
    _d['L0_attn_batch'] = jax.random.normal(jax.random.fold_in(jax.random.key(seed), 1), (16, 1024, 256), dtype=_x0.dtype)
    del _x0
    return _d

def reference(L0_attn_batch, L0_attn_W_qkv, L0_attn_u_qkv, L0_attn_sigma_qkv, L0_attn_W_proj, L0_attn_u_proj, L0_attn_sigma_proj, L0_ffn_weight_fp8, L0_ffn_bias, L0_ffn_input_scale, L0_ffn_weight_scale):

    def _L0_attn_ref(batch, W_qkv, u_qkv, sigma_qkv, W_proj, u_proj, sigma_proj):
        import jax, jax.numpy as jnp
        from jax import lax
        import numpy as np
        DIM = 256
        HEADS = 16
        B, N = (2, 512)

        def sn_dense(x, W, u, sigma_param):
            v = lax.stop_gradient(W @ u)
            v = lax.stop_gradient(v / jnp.linalg.norm(v, ord=2))
            u2 = lax.stop_gradient(W.T @ v)
            u2 = lax.stop_gradient(u2 / jnp.linalg.norm(u2, ord=2))
            sigma = jnp.einsum('c,cd,d->', v, W, u2)
            return x @ (sigma_param[0] / sigma * W)
        b, n, d = batch.shape
        h = HEADS
        hd = d // h
        qkv = sn_dense(batch, W_qkv, u_qkv, sigma_qkv)
        q, k, v = jnp.split(qkv, 3, axis=-1)
        split_heads = lambda t: t.reshape(b, n, h, hd).transpose(0, 2, 1, 3)
        q, k, v = (split_heads(q), split_heads(k), split_heads(v))
        scale = hd ** (-0.5)
        att = jnp.einsum('bhqd,bhkd->bhqk', q, k) * scale
        causal = jnp.tril(jnp.ones((n, n), dtype=jnp.float32))
        big_neg = jnp.finfo(att.dtype).min
        att = jnp.where(causal[None, None] == 0, big_neg, att)
        att = jax.nn.softmax(att, axis=-1)
        x = jnp.einsum('bhqk,bhkd->bhqd', att, v)
        x = x.transpose(0, 2, 1, 3).reshape(b, n, d)
        x = sn_dense(x, W_proj, u_proj, sigma_proj)
        return x

    def _L0_ffn_ref(x, weight_fp8, bias, input_scale, weight_scale):
        import jax, jax.numpy as jnp
        import numpy as np
        FP8_MAX = 448.0
        x_q = jnp.clip(x / input_scale, -FP8_MAX, FP8_MAX)
        x_dq = x_q.astype(jnp.float8_e4m3fn).astype(x.dtype) * input_scale
        w_dq = weight_fp8 * weight_scale
        out = jnp.einsum('bsi,oi->bso', x_dq, w_dq) + bias
        return out
    x = L0_attn_batch
    x = _layernorm(x + _L0_attn_ref(x, L0_attn_W_qkv, L0_attn_u_qkv, L0_attn_sigma_qkv, L0_attn_W_proj, L0_attn_u_proj, L0_attn_sigma_proj), axis=-1)
    x = _layernorm(x + _L0_ffn_ref(x, L0_ffn_weight_fp8, L0_ffn_bias, L0_ffn_input_scale, L0_ffn_weight_scale), axis=-1)
    return x

_drawn_inputs = setup_inputs


def setup_inputs(seed=0):
    import zlib

    import numpy as np

    out = dict(_drawn_inputs(seed))
    spreads = {}
    factors = {}
    for name, (base, spread) in spreads.items():
        noise = np.random.default_rng([zlib.crc32(name.encode()), seed]).standard_normal(out[name].shape)
        drawn = base * np.exp(spread * noise) if base else spread * noise
        out[name] = jnp.asarray(drawn.astype(out[name].dtype))
    for name, factor in factors.items():
        out[name] = (out[name] * factor).astype(out[name].dtype)
    return out
```

```python
import concourse.bass as bass
from concourse import mybir
from contextlib import ExitStack

FP32 = mybir.dt.float32
BF16 = mybir.dt.bfloat16
U32 = mybir.dt.uint32
ALU = mybir.AluOpType
ACT = mybir.ActivationFunctionType
AX = mybir.AxisListType

P = 128
NB, N, D = 16, 1024, 256
H, HD = 16, 16
HG = 4
NG = H // HG
GD = HG * HD
HALF = 512
NT = N // P
HT = HALF // P
KC = D // P
SCALE = float(HD) ** -0.5
EPS = 1e-5
FP8_MAX = 448.0
FP8_MIN_NORMAL = 2.0 ** -6
ROUND_TO_4_BITS = 1.5 * 2.0 ** 20
MASKED = -3.0e38

Q_PARTS = (0, 0, 0, 1, 1, 2)
K_PARTS = (0, 1, 2, 0, 1, 0)
ROWS = len(Q_PARTS) * HD
STACK = ROWS + 3


class Memory:

    def __init__(self, nc, ctx):
        self.nc, self.ctx = nc, ctx

    def sb(self, name, shape, dt=FP32):
        return self.ctx.enter_context(self.nc.sbuf_tensor(name, shape, dt))

    def ps(self, name, shape, dt=FP32):
        return self.ctx.enter_context(self.nc.psum_tensor(name, shape, dt))

    def sem(self, name):
        return self.ctx.enter_context(self.nc.semaphore(name))


def wait_apart(eng, passed, sem, value):
    eng.wait_ge(sem, value)
    eng.sem_inc(passed, 1)


def wait_past(eng, sem, value):
    if not isinstance(value, int) or value > 0:
        eng.wait_ge(sem, value)


def weights_block(nc, mem, W, A):
    with ExitStack() as ctx:
        m = Memory(nc, ctx)
        qkv_raw = m.sb("qkv_raw", [P, KC, 3 * D])
        proj_raw = m.sb("proj_raw", [P, KC, D])
        ffn_raw = m.sb("ffn_raw", [P, KC, D])
        u_qkv = m.sb("u_qkv", [P, 3 * D])
        u_proj = m.sb("u_proj", [P, D])
        scal = m.sb("scal", [P, 4])
        bias_row = m.sb("bias_row", [1, D])
        bias_left = m.sb("bias_left", [1, 2, D])
        bias_parts = m.sb("bias_parts", [1, 3, D], BF16)
        ones = m.sb("ones", [P, P])
        product = m.sb("product", [P, 3 * D])
        wu = m.sb("wu", [P, 2, KC])
        wu_wide = m.sb("wu_wide", [P, 2, KC, P])
        wu_sq = m.sb("wu_sq", [P, 2, KC])
        wtwu = m.sb("wtwu", [P, 4 * D])
        ratio = m.sb("ratio", [P, 2])
        half = m.sb("half", [P, 2])
        norms = m.sb("norms", [P, 4])
        coef = m.sb("coef", [P, 2])
        ffn_t = m.sb("ffn_t", [P, KC, D])
        ffn_left = m.sb("ffn_left", [P, 2, KC, D])
        t_qkv = m.ps("t_qkv", [P, 2, HALF])
        t_proj = m.ps("t_proj", [P, HALF])
        n_ps = m.ps("n_ps", [P, HALF])
        ffn_ps = m.ps("ffn_ps", [P, KC, D])

        loaded = m.sem("w_loaded")
        const_step = m.sem("w_const_step")
        consts = m.sem("w_consts")
        dve_step = m.sem("w_dve_step")
        wu_ready = m.sem("w_wu_ready")
        t_ready = m.sem("w_t_ready")
        ffn_t_ready = m.sem("w_ffn_t_ready")
        ratio_ready = m.sem("w_ratio_ready")
        root_ready = m.sem("w_root_ready")
        parts_ready = m.sem("w_parts_ready")
        bias_placed = m.sem("w_bias_placed")
        loads = 13

        with nc.Block() as block:
            @block.sync
            def _(sp):
                for c in range(KC):
                    rows = slice(c * P, (c + 1) * P)
                    sp.dma_start(qkv_raw[:, c, :], A["W_qkv"][rows, :]).then_inc(loaded, 16)
                    sp.dma_start(proj_raw[:, c, :], A["W_proj"][rows, :]).then_inc(loaded, 16)
                    sp.dma_start(ffn_raw[:, c, :], A["weight"][rows, :]).then_inc(loaded, 16)
                sp.dma_start(u_qkv[:], A["u_qkv"].partition_broadcast(P)).then_inc(loaded, 16)
                sp.dma_start(u_proj[:], A["u_proj"].partition_broadcast(P)).then_inc(loaded, 16)
                for i, name in enumerate(("sigma_qkv", "sigma_proj", "input_scale", "weight_scale")):
                    sp.dma_start(scal[:, i:i + 1], A[name].partition_broadcast(P)).then_inc(loaded, 16)
                sp.dma_start(bias_row[:], A["bias"].partition_broadcast(1)).then_inc(loaded, 16)
                sp.wait_ge(parts_ready, 1)
                sp.wait_ge(consts, 4)
                for i in range(3):
                    sp.dma_start(W["bias3"][i:i + 1, :], bias_parts[0:1, i, :]).then_inc(bias_placed, 16)
                sp.wait_ge(bias_placed, 48)

            @block.gpsimd
            def _(pool):
                pool.memset(W["ident"][:], 0.0).then_inc(const_step, 1)
                pool.memset(W["ident_b"][:], 0.0).then_inc(const_step, 1)
                pool.memset(W["causal"][:], 0.0).then_inc(const_step, 1)
                pool.memset(half[:], 0.5).then_inc(const_step, 1)
                pool.wait_ge(const_step, 3)
                for mat in (W["ident"], W["ident_b"]):
                    pool.affine_select(out=mat[:], in_=mat[:], compare_op=ALU.not_equal, fill=1.0, base=0,
                                       pattern=[[-1, P]], channel_multiplier=1).then_inc(consts, 1)
                pool.affine_select(out=W["causal"][:], in_=W["causal"][:], compare_op=ALU.is_ge, fill=MASKED,
                                   base=0, pattern=[[-1, P]], channel_multiplier=1).then_inc(consts, 1)
                pool.memset(W["bias3"][:], 0.0).then_inc(consts, 1)
                pool.memset(W["minus_half"][:], -0.5)
                pool.memset(W["minus_one"][:], -1.0)
                pool.memset(W["eps"][:], EPS)
                pool.memset(W["ones_b"][:], 1.0)
                pool.wait_ge(ratio_ready, 1)
                pool.wait_ge(const_step, 4)
                pool.tensor_tensor(coef[:], ratio[:], half[:], ALU.pow).then_inc(root_ready, 1)

            @block.tensor
            def _(pe):
                pe.wait_ge(consts, 1)
                pe.wait_ge(loaded, 16 * loads)
                for o in range(KC):
                    for c in range(KC):
                        last = nc.tensor.transpose(ffn_ps[:, c, o * P:(o + 1) * P],
                                                   ffn_raw[:, o, c * P:(c + 1) * P], W["ident"][:])
                last.then_inc(ffn_t_ready, 1)
                pe.wait_ge(wu_ready, 1)
                for c in range(KC):
                    for i in range(2):
                        nc.tensor.matmul(t_qkv[:, i, 0:3 * D // 2], wu_wide[:, 0, c, :],
                                         qkv_raw[:, c, i * 3 * D // 2:(i + 1) * 3 * D // 2],
                                         start=c == 0, stop=c == KC - 1)
                for c in range(KC):
                    nc.tensor.matmul(t_proj[:, 0:D], wu_wide[:, 1, c, :], proj_raw[:, c, :],
                                     start=c == 0, stop=c == KC - 1)
                for c in range(KC):
                    last = nc.tensor.matmul(n_ps[:, 0:2], ones[:], wu_sq[:, :, c],
                                            start=c == 0, stop=c == KC - 1)
                last.then_inc(t_ready, 1)

            @block.vector
            def _(dve):
                steps = [0]

                def step(ins):
                    steps[0] += 1
                    ins.then_inc(dve_step, 1)
                    dve.wait_ge(dve_step, steps[0])

                nc.vector.memset(ones[:], 1.0)
                dve.wait_ge(loaded, 16 * loads)
                for i, (raw, u, n) in enumerate(((qkv_raw, u_qkv, 3 * D), (proj_raw, u_proj, D))):
                    for c in range(KC):
                        step(nc.vector.tensor_tensor_reduce(
                            out=product[:, 0:n], in0=raw[:, c, :], in1=u[:], scale=1.0, scalar=0.0,
                            op0=ALU.mult, op1=ALU.add, accum_out=wu[:, i, c:c + 1]))
                for i in range(2):
                    for c in range(KC):
                        nc.vector.tensor_copy(wu_wide[:, i, c, :], wu[:, i, c:c + 1].to_broadcast([P, P]))
                nc.vector.tensor_tensor(wu_sq[:], wu[:], wu[:], ALU.mult).then_inc(wu_ready, 1)
                dve.wait_ge(ffn_t_ready, 1)
                step(nc.vector.tensor_scalar(ffn_t[:], ffn_ps[:], scal[:, 3:4], scal[:, 2:3], ALU.mult, ALU.mult))
                step(nc.vector.tensor_copy(W["ffn"][:, 0], ffn_t[:]))
                step(nc.vector.tensor_tensor(ffn_left[:, 0], ffn_t[:], W["ffn"][:, 0], ALU.subtract))
                step(nc.vector.tensor_copy(W["ffn"][:, 1], ffn_left[:, 0]))
                nc.vector.tensor_tensor(W["ffn"][:, 2], ffn_left[:, 0], W["ffn"][:, 1], ALU.subtract)
                step(nc.vector.tensor_copy(bias_parts[:, 0], bias_row[:]))
                step(nc.vector.tensor_tensor(bias_left[:, 0], bias_row[:], bias_parts[:, 0], ALU.subtract))
                step(nc.vector.tensor_copy(bias_parts[:, 1], bias_left[:, 0]))
                nc.vector.tensor_tensor(bias_parts[:, 2], bias_left[:, 0], bias_parts[:, 1],
                                        ALU.subtract).then_inc(parts_ready, 1)
                nc.vector.reciprocal(W["inv_input_scale"][:], scal[:, 2:3])
                dve.wait_ge(t_ready, 1)
                for i in range(2):
                    nc.vector.tensor_copy(wtwu[:, i * 3 * D // 2:(i + 1) * 3 * D // 2], t_qkv[:, i, 0:3 * D // 2])
                nc.vector.tensor_copy(norms[:, 2:4], n_ps[:, 0:2])
                step(nc.vector.tensor_copy(wtwu[:, 3 * D:4 * D], t_proj[:, 0:D]))
                step(nc.vector.tensor_tensor_reduce(
                    out=product[:, 0:3 * D], in0=wtwu[:, 0:3 * D], in1=wtwu[:, 0:3 * D], scale=1.0, scalar=0.0,
                    op0=ALU.mult, op1=ALU.add, accum_out=norms[:, 0:1]))
                step(nc.vector.tensor_tensor_reduce(
                    out=product[:, 0:D], in0=wtwu[:, 3 * D:4 * D], in1=wtwu[:, 3 * D:4 * D], scale=1.0, scalar=0.0,
                    op0=ALU.mult, op1=ALU.add, accum_out=norms[:, 1:2]))
                step(nc.vector.reciprocal(ratio[:], norms[:, 0:2]))
                nc.vector.tensor_tensor(ratio[:], ratio[:], norms[:, 2:4], ALU.mult).then_inc(ratio_ready, 1)
                dve.wait_ge(root_ready, 1)
                step(nc.vector.tensor_tensor(coef[:], coef[:], scal[:, 0:2], ALU.mult))
                for c in range(KC):
                    for part in range(2):
                        nc.vector.tensor_scalar(
                            W["qk"][:, c, :, part * GD:(part + 1) * GD],
                            qkv_raw[:, c, part * D:(part + 1) * D].rearrange("p (g d) -> p g d", g=NG),
                            coef[:, 0:1], None, ALU.mult)
                    nc.vector.tensor_scalar(W["v"][:, c, :], qkv_raw[:, c, 2 * D:3 * D], coef[:, 0:1], None, ALU.mult)
                    nc.vector.tensor_scalar(W["proj"][:, c, :], proj_raw[:, c, :], coef[:, 1:2], None, ALU.mult)


def project_block(nc, W, A, S, T, nb):
    with ExitStack() as ctx:
        m = Memory(nc, ctx)
        x_in = [m.sb(f"p_x{h}", [P, HT, D]) for h in range(2)]
        x_t = [m.sb(f"p_xt{h}", [P, KC, HALF]) for h in range(2)]
        parts = [m.sb(f"p_parts{h}", [P, 3, NG, HALF], BF16) for h in range(2)]
        left = [m.sb(f"p_left{i}", [P, HALF]) for i in range(2)]
        v_out = [m.sb(f"p_v{h}", [P, NG, HT, GD]) for h in range(2)]
        xt_ps = [m.ps(f"p_xtp{c}", [P, HALF]) for c in range(KC)]
        qk_ps = [m.ps(f"p_qkp{i}", [P, HALF]) for i in range(2)]
        v_ps = [m.ps(f"p_vp{i}", [P, HT // 2, D]) for i in range(2)]

        x_loaded = [m.sem(f"p_x_loaded{h}") for h in range(2)]
        xt_ready = m.sem("p_xt_ready")
        xt_by_act = m.sem("p_xt_by_act")
        xt_by_dve = m.sem("p_xt_by_dve")
        qk_ready = m.sem("p_qk_ready")
        hi_ready = m.sem("p_hi_ready")
        left_ready = m.sem("p_left_ready")
        mid_ready = m.sem("p_mid_ready")
        lo_ready = m.sem("p_lo_ready")
        v_ready = m.sem("p_v_ready")
        v_copied = m.sem("p_v_copied")
        stored = [m.sem(f"p_stored{h}") for h in range(2)]
        stores = 16 * 4

        with nc.Block() as block:
            @block.sync
            def _(sp):
                def load(b, h):
                    rows = A["x"][bass.ds(b * N + h * HALF, HALF), :]
                    sp.dma_start(x_in[h][:], rows.rearrange("(t p) d -> p t d", p=P)).then_inc(x_loaded[h], 16)

                def store(n, b, h):
                    cols = slice(h * HALF, (h + 1) * HALF)
                    sp.wait_ge(lo_ready, NG * (n + 1))
                    for part in range(3):
                        sp.dma_start(S["qk"][bass.ds(b, 1), :, part, :, cols].rearrange("a g r n -> r (a g) n"),
                                     parts[h][:, part]).then_inc(stored[h], 16)
                    sp.wait_ge(v_copied, 2 * n + 2)
                    sp.dma_start(
                        S["v"][bass.ds(b, 1), :, :, h * HT * GD:(h + 1) * HT * GD].rearrange("a g p n -> p (a g) n"),
                        v_out[h][:].rearrange("p g t d -> p g (t d)")).then_inc(stored[h], 16)

                for h in range(2):
                    sp.sem_inc(stored[h], 16)
                    load(0, h)
                with sp.Fori(0, nb - 1) as b:
                    for h in range(2):
                        sp.wait_ge(xt_ready, KC * (2 * b + h + 1))
                        load(b + 1, h)
                        store(2 * b + h, b, h)
                for h in range(2):
                    sp.wait_ge(stored[h], stores + 16)
                for g in range(2):
                    load_stacks(sp, S, T, 0, g)
                    load_v(sp, S, T, 0, g)
                store(2 * nb - 2, nb - 1, 0)
                store(2 * nb - 1, nb - 1, 1)
                for h in range(2):
                    sp.wait_ge(stored[h], stores * nb + 16)

            @block.tensor
            def _(pe):
                def transpose_x(n, b, h):
                    pe.wait_ge(x_loaded[h], 16 * (b + 1))
                    for c in range(KC):
                        wait_past(pe, (xt_by_act, xt_by_dve)[c], n)
                        for t in range(HT):
                            last = nc.tensor.transpose(xt_ps[c][:, t * P:(t + 1) * P],
                                                       x_in[h][:, t, c * P:(c + 1) * P], W["ident"][:])
                        last.then_inc(xt_ready, 1)

                def half(n, b, h, last_half=False):
                    pe.wait_ge(xt_by_act, n + 1)
                    pe.wait_ge(xt_by_dve, n + 1)
                    for g in range(NG):
                        wait_past(pe, left_ready, NG * n + g - 1)
                        for c in range(KC):
                            last = nc.tensor.matmul(qk_ps[g % 2][:], W["qk"][:, c, g, :], x_t[h][:, c, :],
                                                    start=c == 0, stop=c == KC - 1)
                        last.then_inc(qk_ready, 1)
                    if not last_half:
                        transpose_x(n + 1, b + h, 1 - h)
                    for i in range(2):
                        wait_past(pe, v_copied, 2 * n + i - 1)
                        for t in (2 * i, 2 * i + 1):
                            for c in range(KC):
                                last = nc.tensor.matmul(v_ps[i][:, t % 2, :], x_t[h][:, c, t * P:(t + 1) * P],
                                                        W["v"][:, c, :], start=c == 0, stop=c == KC - 1)
                        last.then_inc(v_ready, 1)

                transpose_x(0, 0, 0)
                half(0, 0, 0)
                half(1, 0, 1)
                with pe.Fori(1, nb - 1) as b:
                    for h in range(2):
                        half(2 * b + h, b, h)
                half(2 * nb - 2, nb - 1, 0)
                half(2 * nb - 1, nb - 1, 1, last_half=True)

            def over_halves(eng, half):
                for h in range(2):
                    half(h, 0, h)
                with eng.Fori(1, nb) as b:
                    for h in range(2):
                        half(2 * b + h, b, h)

            @block.scalar
            def _(act):
                def copy_xt(n, h):
                    act.wait_ge(xt_ready, KC * n + 1)
                    wait_past(act, v_copied, 2 * (n - 1))
                    nc.scalar.activation(x_t[h][:, 0, :], xt_ps[0][:], ACT.Copy).then_inc(xt_by_act, 1)

                def half(n, b, h):
                    copy_xt(n, h)
                    wait_past(act, stored[h], stores * b + 16)
                    for g in range(NG):
                        act.wait_ge(qk_ready, NG * n + g + 1)
                        nc.scalar.activation(parts[h][:, 0, g, :], qk_ps[g % 2][:], ACT.Copy).then_inc(hi_ready, 1)
                        act.wait_ge(left_ready, NG * n + g + 1)
                        nc.scalar.activation(parts[h][:, 1, g, :], left[g % 2][:], ACT.Copy).then_inc(mid_ready, 1)

                over_halves(act, half)

            @block.vector
            def _(dve):
                def half(n, b, h):
                    dve.wait_ge(xt_ready, KC * n + 2)
                    nc.vector.tensor_copy(x_t[h][:, 1, :], xt_ps[1][:]).then_inc(xt_by_dve, 1)
                    if not isinstance(n, int) or n > 0:
                        copy_v(n - 1, b if h else b - 1, 1 - h)
                    for g in range(NG):
                        dve.wait_ge(hi_ready, NG * n + g + 1)
                        wait_past(dve, lo_ready, NG * n + g - 1)
                        nc.vector.tensor_tensor(left[g % 2][:], qk_ps[g % 2][:], parts[h][:, 0, g, :],
                                                ALU.subtract).then_inc(left_ready, 1)

                def copy_v(n, b, h):
                    wait_past(dve, stored[h], stores * b + 16)
                    for i in range(2):
                        dve.wait_ge(v_ready, 2 * n + i + 1)
                        nc.vector.tensor_copy(
                            v_out[h][:, :, 2 * i:2 * i + 2, :],
                            v_ps[i][:].rearrange("p t (g d) -> p g t d", g=NG)).then_inc(v_copied, 1)

                over_halves(dve, half)
                copy_v(2 * nb - 1, nb - 1, 1)

            @block.gpsimd
            def _(pool):
                def half(n, b, h):
                    wait_past(pool, stored[h], stores * b + 16)
                    for g in range(NG):
                        pool.wait_ge(mid_ready, NG * n + g + 1)
                        nc.gpsimd.tensor_tensor(parts[h][:, 2, g, :], left[g % 2][:], parts[h][:, 1, g, :],
                                                ALU.subtract).then_inc(lo_ready, 1)

                over_halves(pool, half)


STEPS = [(c, kt) for c in range(2) for kt in range(HT * (c + 1))]
NS = len(STEPS)
FIRST = {c: STEPS.index((c, 0)) for c in range(2)}
LAST = {c: FIRST[c] + HT * (c + 1) - 1 for c in range(2)}
PROBS = 4
STEP_OVERHEAD = 128
LAG = 2
SPREAD_AT = 5
RING = 3


def diagonal(s):
    c, kt = STEPS[s]
    return kt >= HT * c


N_DIAG = sum(diagonal(s) for s in range(NS))


def diag_index(s):
    return sum(diagonal(i) for i in range(s))


def step_columns(s):
    c, kt = STEPS[s]
    first = max(c * HALF, kt * P)
    return first, (c + 1) * HALF - first


def maxima_jobs():
    out = []
    for qt in range(NT):
        keys = (qt + 1) * P
        for k0 in range(0, keys, HALF):
            n = min(HALF, keys - k0)
            per = min(HG, HALF // n)
            out += [(qt, h, per, k0, n) for h in range(0, HG, per)]
    return out


MAXIMA = maxima_jobs()
MAXIMA_HALF = sum(qt < HT for qt, *_ in MAXIMA)


def job_list():
    out = [("max", 1, i) for i in range(len(MAXIMA))]
    out.insert(23, ("out", 0, 0))
    out.insert(MAXIMA_HALF + 3, ("shift", 1, 0))
    out.insert(10, ("out", -1, 1))
    out.insert(3, ("shift", 0, 1))
    return out


JOBS = len(job_list())


def number_jobs(events, start):
    out = []
    for e in events:
        if e[0] in ("max", "shift", "out"):
            e, start = e + (start,), start + 1
        out.append(e)
        if e[0] == "max" and e[2] == MAXIMA_HALF - 1:
            out.append(("split", e[1], 0, e[3]))
        if e[0] == "max" and e[2] == len(MAXIMA) - 1:
            out.append(("split", e[1], 1, e[3]))
    return out, start


def group_events(u, first=False, last=False):
    cost = {"max": lambda i: MAXIMA[i][2] * MAXIMA[i][4] + 64, "out": lambda c: 700, "shift": lambda c: 350}
    todo = job_list()
    jobs_cost = sum(cost[kind](x) for kind, _, x in todo)
    steps_cost = sum(3 * (step_columns(s)[1] + STEP_OVERHEAD) for s in range(NS))
    jobs_spent = steps_spent = 0
    out = [("begin", u, 0)]

    def lay_jobs():
        nonlocal jobs_spent
        while todo and jobs_spent * steps_cost <= steps_spent * jobs_cost:
            kind, du, x = todo[0]
            missing = (du < 0 and first) or (du > 0 and last)
            if kind == "out" and not missing and ("evacuate", u + du, x) not in out:
                break
            todo.pop(0)
            jobs_spent += cost[kind](x)
            if not missing:
                out.append((kind, u + du, x))

    for s in range(NS):
        if s == SPREAD_AT:
            out.append(("spread", u, 0))
        for pair in range(2):
            out.append(("scores", u, s, pair))
            steps_spent += step_columns(s)[1] + STEP_OVERHEAD
            lay_jobs()
        if s >= LAG or not first:
            behind = (s - LAG) % NS
            du = 0 if s >= LAG else -1
            out.append(("values", u + du, behind))
            out += [("evacuate", u + du, c) for c in range(2) if behind == LAST[c]]
        steps_spent += step_columns(s)[1] + STEP_OVERHEAD
    steps_spent = steps_cost + 1
    lay_jobs()
    return out


def load_stacks(eng, S, T, b, g):
    for r in range(len(Q_PARTS)):
        rows = slice(r * HD, (r + 1) * HD)
        for stack, part, first in ((T["k_stack"], K_PARTS[r], GD), (T["q_stack"], Q_PARTS[r], 0)):
            src = S["qk"][bass.ds(b, 1), g, part, first:first + GD, :]
            eng.dma_start(stack[g][rows, :, :], src.rearrange("a (h d) n -> (a d) h n", h=HG)
                          ).then_inc(T["stack_loaded"][g], 16)


def load_v(eng, S, T, b, g):
    src = S["v"][bass.ds(b, 1), g].rearrange("a p n -> (a p) n")
    eng.dma_start(T["v_in"][g % 2][:].rearrange("p t d -> p (t d)"), src).then_inc(T["v_loaded"][g % 2], 16)


def attend_block(nc, W, S, T, nb):
    loops = nb - 1
    with ExitStack() as ctx:
        m = Memory(nc, ctx)
        q_stack, k_stack, v_in = T["q_stack"], T["k_stack"], T["v_in"]
        stack_loaded, v_loaded = T["stack_loaded"], T["v_loaded"]
        v_ones = [m.sb(f"a_v{i}", [P, NT, HG, 2 * HD]) for i in range(2)]
        probs = [m.sb(f"a_probs{i}", [P, HG, HALF]) for i in range(PROBS)]
        neg_max = m.sb("a_neg_max", [P, NT, HG])
        neg_part = m.sb("a_neg_part", [P, 2, HT, HG])
        neg_left = m.sb("a_neg_left", [P, 2, HT, HG])
        shift = m.sb("a_shift", [P, NT, HG, 3], BF16)
        shift_t = [m.sb(f"a_shift_t{c}", [HG * 3, HALF], BF16) for c in range(2)]
        out_t = [m.sb(f"a_out_t{c}", [P, HALF]) for c in range(2)]
        inv_sum = [m.sb(f"a_inv{c}", [P, HT, HG]) for c in range(2)]
        out_n = [m.sb(f"a_out_n{c}", [P, HT, HG, HD]) for c in range(2)]
        s_ps = [m.ps(f"a_s{i}", [P, 2, HALF]) for i in range(2)]
        pv_ps = m.ps("a_pv", [P, HALF])
        ring = [m.ps(f"a_ring{i}", [P, HALF]) for i in range(RING)]

        scores_ready = m.sem("a_scores_ready")
        exp_done = m.sem("a_exp_done")
        causal_done = m.sem("a_causal_done")
        values_done = m.sem("a_values_done")
        evacuated = m.sem("a_evacuated")
        ring_full = m.sem("a_ring_full")
        ring_free = m.sem("a_ring_free")
        maxima_ready = m.sem("a_maxima_ready")
        split_step = m.sem("a_split_step")
        shift_loaded = [m.sem(f"a_shift_loaded{c}") for c in range(2)]
        v_spread = m.sem("a_v_spread")
        inv_ready = m.sem("a_inv_ready")
        out_stored = [m.sem(f"a_out_stored{c}") for c in range(2)]
        passed = m.sem("a_passed")
        k_ones_ready = m.sem("a_k_ones_ready")
        v_ones_ready = m.sem("a_v_ones_ready")
        stack_load = 16 * (len(Q_PARTS) + len(K_PARTS))
        shift_load = 16 * HG

        prologue = [("begin", -1, 0), ("spread", -1, 0)]
        prologue += [("max", 0, i) for i in range(MAXIMA_HALF + 3)] + [("shift", 0, 0)]
        prologue += [("max", 0, i) for i in range(MAXIMA_HALF + 3, len(MAXIMA))]
        prologue += group_events(0, first=True)
        body = [e for u in range(1, NG + 1) for e in group_events(u)]
        epilogue = [e for u in range(1, NG) for e in group_events(u, last=u == NG - 1)]
        epilogue += [("values", NG - 1, s) for s in range(NS - LAG, NS)]
        epilogue += [("evacuate", NG - 1, 1), ("out", NG - 1, 1)]
        prologue, at_loop = number_jobs(prologue, 0)
        body, at_next = number_jobs(body, at_loop)
        epilogue, _ = number_jobs(epilogue, at_loop)
        assert at_next - at_loop == NG * JOBS and NG * JOBS % RING == 0

        def run(eng, handle):
            for e in prologue:
                handle(e, 0)
            with eng.Fori(0, loops) as it:
                for e in body:
                    handle(e, it)
            for e in epilogue:
                handle(e, loops)

        with nc.Block() as block:
            @block.sync
            def _(sp):
                def load_later_group(u, it):
                    load_stacks(sp, S, T, it + u // NG, u % NG)
                    if u >= 2 or not isinstance(it, int) or it > 0:
                        sp.wait_ge(v_spread, NG * it + u - 1)
                    load_v(sp, S, T, it + u // NG, u % NG)

                def handle(e, it):
                    kind, u, x = e[:3]
                    if kind == "begin":
                        ahead = u + 2
                        if u >= 0 and not (isinstance(it, int) and it == loops and ahead >= NG):
                            if isinstance(it, int) and it == 0 and u < 1:
                                load_later_group(ahead, it)
                            else:
                                sp.wait_ge(scores_ready, 2 * NS * (NG * it + u - 1) + 1)
                                load_later_group(ahead, it)
                    if kind == "shift":
                        sp.wait_ge(ring_free, NG * JOBS * it + e[3] + 1)
                        for h in range(HG):
                            sp.dma_start(q_stack[u % NG][ROWS:STACK, h, x * HALF:(x + 1) * HALF],
                                         shift_t[x][3 * h:3 * h + 3, :]).then_inc(shift_loaded[x], 16)
                    if kind == "out":
                        sp.wait_ge(ring_free, NG * JOBS * it + e[3] + 1)
                        b, g = it + u // NG, u % NG
                        dst = S["out"][bass.ds(b, 1), x, :, :, g * GD:(g + 1) * GD].rearrange("a p t n -> (a p) t n")
                        sp.dma_start(dst, out_n[x][:].rearrange("p t h d -> p t (h d)")).then_inc(out_stored[x], 16)

                run(sp, handle)
                for c in range(2):
                    sp.wait_ge(out_stored[c], 16 * NG * nb + 16)

            @block.tensor
            def _(pe):
                def handle(e, it):
                    kind, u, x = e[:3]
                    group = NG * it + u
                    buf = u % NG
                    start_of_all = isinstance(it, int) and it == 0 and u == 0
                    if kind == "scores":
                        s, pair = x, e[3]
                        first, cols = step_columns(s)
                        c, kt = STEPS[s]
                        if isinstance(it, int) and it == 0 and s == 0 and pair == 0:
                            pe.wait_ge(k_ones_ready, NG)
                            pe.wait_ge(v_ones_ready, 1)
                        if kt == 0 and pair == 0:
                            pe.wait_ge(shift_loaded[c], shift_load * (group + 1))
                        if not (start_of_all and s == 0):
                            pe.wait_ge(exp_done, 2 * NS * group + 2 * s + pair - 1)
                        for i in range(2):
                            h = 2 * pair + i
                            last = nc.tensor.matmul(s_ps[pair][:, i, 0:cols],
                                                    k_stack[buf][0:STACK, h, kt * P:(kt + 1) * P],
                                                    q_stack[buf][0:STACK, h, first:first + cols],
                                                    start=True, stop=True)
                        last.then_inc(scores_ready, 1)
                    if kind == "values":
                        s = x
                        c, kt = STEPS[s]
                        first, cols = step_columns(s)
                        if s == 0:
                            pe.wait_ge(v_spread, group + 1)
                        if kt == 0 and not (start_of_all and c == 0):
                            pe.wait_ge(evacuated, 2 * group + c)
                        pe.wait_ge(exp_done, 2 * NS * group + 2 * s + 2)
                        if diagonal(s):
                            pe.wait_ge(causal_done, N_DIAG * group + diag_index(s) + 1)
                        at = first - c * HALF
                        for h in range(HG):
                            last = nc.tensor.matmul(pv_ps[32 * h:32 * h + 32, at:at + cols],
                                                    v_ones[u % 2][:, kt, h, :], probs[s % PROBS][:, h, 0:cols],
                                                    start=kt == 0, stop=s == LAST[c])
                        last.then_inc(values_done, 1)
                    if kind in ("max", "shift", "out"):
                        number = NG * JOBS * it + e[3]
                        bank = ring[e[3] % RING]
                        if not (isinstance(number, int) and number < RING):
                            pe.wait_ge(ring_free, number - RING + 1)
                    if kind == "max":
                        if x == 0:
                            pe.wait_ge(stack_loaded[buf], stack_load * (it + u // NG + 1))
                        qt, h0, heads, k0, n = MAXIMA[x]
                        masked = k0 + n == (qt + 1) * P
                        for h in range(heads):
                            last = nc.tensor.matmul(bank[:, h * n:(h + 1) * n],
                                                    q_stack[buf][0:ROWS, h0 + h, qt * P:(qt + 1) * P],
                                                    k_stack[buf][0:ROWS, h0 + h, k0:k0 + n],
                                                    start=h == 0, stop=h == heads - 1 and not masked)
                        if masked:
                            diagonals = bank[:, 0:heads * n].rearrange("p (h k) -> p h k", h=heads)[:, :, n - P:n]
                            last = nc.tensor.matmul(diagonals, W["ident_b"][:],
                                                    W["causal"][:].unsqueeze(1).to_broadcast([P, heads, P]),
                                                    start=False, stop=True)
                        last.then_inc(ring_full, 1)
                    if kind == "shift":
                        pe.wait_ge(split_step, 4 * (2 * group + x + 1))
                        for t in range(HT):
                            last = nc.tensor.transpose(bank[:].bitcast(BF16)[0:3 * HG, t * P:(t + 1) * P],
                                                       shift[:, x * HT + t, :, :].rearrange("p h k -> p (h k)"),
                                                       W["ident_b"][:])
                        last.then_inc(ring_full, 1)
                    if kind == "out":
                        pe.wait_ge(evacuated, 2 * group + x + 1)
                        for t in range(HT):
                            last = nc.tensor.transpose(bank[:, t * P:(t + 1) * P], out_t[x][:, t * P:(t + 1) * P],
                                                       W["ident"][:])
                        last.then_inc(ring_full, 1)

                run(pe, handle)

            @block.scalar
            def _(act):
                def handle(e, it):
                    kind, u, x = e[:3]
                    group = NG * it + u
                    start_of_all = isinstance(it, int) and it == 0 and u == 0
                    if kind == "scores":
                        s, pair = x, e[3]
                        _, cols = step_columns(s)
                        act.wait_ge(scores_ready, 2 * NS * group + 2 * s + pair + 1)
                        if pair == 0 and not (start_of_all and s < PROBS):
                            act.wait_ge(values_done, NS * group + s - PROBS + 1)
                        nc.scalar.activation(probs[s % PROBS][:, 2 * pair:2 * pair + 2, 0:cols],
                                             s_ps[pair][:, :, 0:cols], ACT.Exp, scale=SCALE).then_inc(exp_done, 1)
                    if kind == "evacuate":
                        c = x
                        act.wait_ge(values_done, NS * group + LAST[c] + 1)
                        if not start_of_all:
                            act.wait_ge(inv_ready, 2 * group + c)
                        nc.scalar.activation(out_t[c][:], pv_ps[:], ACT.Copy).then_inc(evacuated, 1)

                for i in range(NG):
                    nc.scalar.activation(k_stack[i][ROWS:STACK, :, :],
                                         W["ones_b"][ROWS:STACK, 0:1].unsqueeze(2).to_broadcast([3, HG, N]),
                                         ACT.Copy).then_inc(k_ones_ready, 1)
                run(act, handle)

            @block.vector
            def _(dve):
                def handle(e, it):
                    kind, u, x = e[:3]
                    group = NG * it + u
                    start_of_all = isinstance(it, int) and it == 0 and u == 0
                    if kind in ("max", "shift", "out"):
                        number = NG * JOBS * it + e[3]
                        bank = ring[e[3] % RING]
                        dve.wait_ge(ring_full, number + 1)
                    if kind == "max":
                        qt, h0, heads, k0, n = MAXIMA[x]
                        if qt == 0 and not start_of_all:
                            dve.wait_ge(split_step, 4 * (2 * group - 1))
                        heads_of = slice(h0, h0 + heads)
                        to = neg_max[:, qt, heads_of] if qt < HT else neg_part[:, k0 // HALF, qt - HT, heads_of]
                        nc.vector.tensor_reduce(to, bank[:, 0:heads * n].rearrange("p (h k) -> p h k", h=heads),
                                                AX.X, ALU.max, negate=True).then_inc(ring_free, 1)
                        if x == len(MAXIMA) - 1:
                            if not start_of_all:
                                dve.wait_ge(split_step, 4 * 2 * group)
                            dve.wait_ge(ring_free, number + 1)
                            nc.vector.tensor_tensor(neg_max[:, HT:NT, :], neg_part[:, 0], neg_part[:, 1],
                                                    ALU.min).then_inc(maxima_ready, 1)
                    if kind == "shift":
                        if not start_of_all:
                            dve.wait_ge(shift_loaded[x], shift_load * group)
                        nc.vector.tensor_copy(shift_t[x][:], bank[:].bitcast(BF16)[0:3 * HG, 0:HALF]
                                              ).then_inc(ring_free, 1)
                    if kind == "out":
                        view = bank[:].rearrange("p (t h d) -> p t h d", t=HT, h=HG)
                        nc.vector.reciprocal(inv_sum[x][:], view[:, :, :, HD]).then_inc(inv_ready, 1)
                        if not start_of_all:
                            dve.wait_ge(out_stored[x], 16 * group + 16)
                        dve.wait_ge(inv_ready, 2 * group + x + 2)
                        nc.vector.tensor_tensor(out_n[x][:], view[:, :, :, 0:HD],
                                                inv_sum[x][:].unsqueeze(3).to_broadcast([P, HT, HG, HD]),
                                                ALU.mult).then_inc(ring_free, 1)

                dve.sem_inc(inv_ready, 1)
                for c in range(2):
                    dve.sem_inc(out_stored[c], 16)
                run(dve, handle)

            @block.gpsimd
            def _(pool):
                def handle(e, it):
                    kind, u, x = e[:3]
                    group = NG * it + u
                    start_of_all = isinstance(it, int) and it == 0 and u == 0
                    if kind == "spread" and not (isinstance(it, int) and it == loops and u == NG - 1):
                        if not (isinstance(it, int) and it == 0 and u < 1):
                            pool.wait_ge(values_done, NS * group)
                        wait_apart(pool, passed, v_loaded[(u + 1) % 2], 16 * (NG // 2 * it + (u + 1) // 2 + 1))
                        nc.gpsimd.tensor_copy(v_ones[(u + 1) % 2][:, :, :, 0:HD],
                                              v_in[(u + 1) % 2][:].rearrange("p t (h d) -> p t h d", h=HG)
                                              ).then_inc(v_spread, 1)
                    if kind == "scores" and e[3] == 1 and diagonal(x):
                        wait_apart(pool, passed, exp_done, 2 * NS * group + 2 * x + 2)
                        block_ = probs[x % PROBS][:, :, 0:P]
                        nc.gpsimd.affine_select(out=block_, in_=block_, compare_op=ALU.is_ge, fill=0.0, base=0,
                                                pattern=[[0, HG], [1, P]], channel_multiplier=-1
                                                ).then_inc(causal_done, 1)
                    if kind == "split":
                        steps = 4 * (2 * group + x)
                        if not start_of_all:
                            pool.wait_ge(shift_loaded[x], shift_load * group)
                        if x == 0:
                            wait_apart(pool, passed, ring_free, NG * JOBS * it + e[3] + 1)
                        else:
                            wait_apart(pool, passed, maxima_ready, group + 1)
                        tiles = slice(x * HT, (x + 1) * HT)
                        part = [shift[:, tiles, :, i] for i in range(3)]
                        nc.gpsimd.tensor_copy(part[0], neg_max[:, tiles]).then_inc(split_step, 1)
                        pool.wait_ge(split_step, steps + 1)
                        nc.gpsimd.tensor_tensor(neg_left[:, x], neg_max[:, tiles], part[0],
                                                ALU.subtract).then_inc(split_step, 1)
                        wait_apart(pool, passed, split_step, steps + 2)
                        nc.gpsimd.tensor_copy(part[1], neg_left[:, x]).then_inc(split_step, 1)
                        pool.wait_ge(split_step, steps + 3)
                        nc.gpsimd.tensor_tensor(part[2], neg_left[:, x], part[1], ALU.subtract).then_inc(split_step, 1)

                for i in range(2):
                    last = nc.gpsimd.memset(v_ones[i][:, :, :, HD:2 * HD], 1.0)
                last.then_inc(v_ones_ready, 1)
                run(pool, handle)


def finish_block(nc, W, A, S, nb):
    with ExitStack() as ctx:
        m = Memory(nc, ctx)
        two = range(2)
        o_in = [m.sb(f"f_o{h}", [P, HT, D]) for h in two]
        x_in = [m.sb(f"f_x{h}", [P, HT, D]) for h in two]
        o_t = [m.sb(f"f_ot{h}", [P, KC, HALF]) for h in two]
        y1 = [m.sb(f"f_y1{h}", [P, HT, D]) for h in two]
        x1 = [m.sb(f"f_x1{h}", [P, HT, D]) for h in two]
        scaled = [m.sb(f"f_scaled{h}", [P, HT, D]) for h in two]
        clipped = [m.sb(f"f_clipped{h}", [P, HT, D]) for h in two]
        power = m.sb("f_power", [P, HT, D])
        magic = [m.sb(f"f_magic{h}", [P, HT, D]) for h in two]
        shifted = m.sb("f_shifted", [P, HT, D])
        x_q = [m.sb(f"f_xq{h}", [P, HT, D], BF16) for h in two]
        x_qt = [m.sb(f"f_xqt{h}", [P, KC, HALF], BF16) for h in two]
        y2 = [m.sb(f"f_y2{h}", [P, HT, D]) for h in two]
        result = [m.sb(f"f_result{h}", [P, HT, D]) for h in two]
        stats = [m.sb(f"f_stats{i}", [P, HT, 6]) for i in two]
        mean_var = [m.sb(f"f_mv{i}", [P, HT, 2]) for i in two]
        var_eps = [m.sb(f"f_ve{i}", [P, HT]) for i in two]
        rstd = [m.sb(f"f_rstd{i}", [P, HT]) for i in two]
        neg_mean = m.sb("f_neg_mean", [P, HT])
        offset = m.sb("f_offset", [P, HT])
        o_ps = [m.ps(f"f_ops{c}", [P, HALF]) for c in range(KC)]
        proj_ps = m.ps("f_projps", [P, HT, D])
        q_ps = m.ps("f_qps", [P, KC, HALF], BF16)
        ffn_ps = m.ps("f_ffnps", [P, HT, D])

        passed = m.sem("f_passed")
        loaded = [m.sem(f"f_loaded{h}") for h in two]
        ot_ready = m.sem("f_ot_ready")
        ot_copied = m.sem("f_ot_copied")
        proj_ready = m.sem("f_proj_ready")
        y1_ready = m.sem("f_y1_ready")
        stats_ready = [m.sem(f"f_stats_ready{i}") for i in two]
        mv_ready = [m.sem(f"f_mv_ready{i}") for i in two]
        eps_added = [m.sem(f"f_eps_added{i}") for i in two]
        rstd_ready = [m.sem(f"f_rstd_ready{i}") for i in two]
        x1_ready = m.sem("f_x1_ready")
        scaled_ready = m.sem("f_scaled_ready")
        clipped_ready = m.sem("f_clipped_ready")
        power_ready = m.sem("f_power_ready")
        magic_ready = m.sem("f_magic_ready")
        shifted_ready = m.sem("f_shifted_ready")
        xq_ready = m.sem("f_xq_ready")
        qt_ready = m.sem("f_qt_ready")
        qt_copied = m.sem("f_qt_copied")
        ffn_ready = m.sem("f_ffn_ready")
        y2_ready = m.sem("f_y2_ready")
        offset_ready = m.sem("f_offset_ready")
        result_ready = m.sem("f_result_ready")
        stored = [m.sem(f"f_stored{h}") for h in two]

        def run(eng, parts):
            most = 3

            def turn(b, h):
                for ahead, function in parts:
                    n = 2 * b + h + ahead
                    if not isinstance(n, int) or 0 <= n < 2 * nb:
                        function(n, b + (h + ahead) // 2, (h + ahead) % 2)

            for i in range(-most, 2):
                turn(i // 2, i % 2)
            with eng.Fori(1, nb - 2) as b:
                for h in two:
                    turn(b, h)
            for i in range(2 * nb - 4, 2 * nb + 1):
                turn(i // 2, i % 2)

        with nc.Block() as block:
            @block.sync
            def _(sp):
                def load(n, b, h):
                    wait_past(sp, y1_ready, n - 1)
                    src = A["x"][bass.ds(b * N + h * HALF, HALF), :]
                    sp.dma_start(x_in[h][:], src.rearrange("(t p) d -> p t d", p=P)).then_inc(loaded[h], 16)
                    src = S["out"][bass.ds(b, 1), h].rearrange("a p t d -> (a p) t d")
                    sp.dma_start(o_in[h][:], src).then_inc(loaded[h], 16)

                run(sp, [(3, load)])

            @block.tensor
            def _(pe):
                def transpose_output(n, b, h):
                    pe.wait_ge(loaded[h], 32 * (b + 1))
                    wait_past(pe, ot_copied, KC * n)
                    for c in range(KC):
                        for t in range(HT):
                            last = nc.tensor.transpose(o_ps[c][:, t * P:(t + 1) * P],
                                                       o_in[h][:, t, c * P:(c + 1) * P], W["ident"][:])
                        last.then_inc(ot_ready, 1)

                def project(n, b, h):
                    wait_past(pe, y1_ready, n)
                    pe.wait_ge(ot_copied, KC * (n + 1))
                    for t in range(HT):
                        for c in range(KC):
                            last = nc.tensor.matmul(proj_ps[:, t, :], o_t[h][:, c, t * P:(t + 1) * P],
                                                    W["proj"][:, c, :], start=c == 0, stop=c == KC - 1)
                    last.then_inc(proj_ready, 1)

                def transpose_rounded(n, b, h):
                    wait_past(pe, qt_copied, n)
                    pe.wait_ge(xq_ready, n + 1)
                    for c in range(KC):
                        for t in range(HT):
                            last = nc.tensor.transpose(q_ps[:, c, t * P:(t + 1) * P],
                                                       x_q[h][:, t, c * P:(c + 1) * P], W["ident_b"][:])
                    last.then_inc(qt_ready, 1)

                def linear(n, b, h):
                    wait_past(pe, y2_ready, n)
                    pe.wait_ge(qt_copied, n + 1)
                    for t in range(HT):
                        nc.tensor.matmul(ffn_ps[:, t, :], W["ones_b"][:], W["bias3"][:], start=True, stop=False)
                        for c in range(KC):
                            for part in range(3):
                                last = nc.tensor.matmul(ffn_ps[:, t, :], x_qt[h][:, c, t * P:(t + 1) * P],
                                                        W["ffn"][:, part, c, :], start=False,
                                                        stop=(c, part) == (KC - 1, 2))
                    last.then_inc(ffn_ready, 1)

                run(pe, [(2, project), (0, transpose_rounded), (3, transpose_output), (0, linear)])

            @block.scalar
            def _(act):
                def copy_output(n, b, h):
                    wait_past(act, proj_ready, n - 1)
                    for c in range(KC):
                        act.wait_ge(ot_ready, KC * n + c + 1)
                        nc.scalar.activation(o_t[h][:, c, :], o_ps[c][:], ACT.Copy).then_inc(ot_copied, 1)

                def scale_input(n, b, h):
                    act.wait_ge(x1_ready, n + 1)
                    wait_past(act, clipped_ready, n - 1)
                    nc.scalar.activation(scaled[h][:], x1[h][:], ACT.Copy, scale=W["inv_input_scale"][:, 0:1]
                                         ).then_inc(scaled_ready, 1)

                def copy_rounded(n, b, h):
                    act.wait_ge(qt_ready, n + 1)
                    nc.scalar.activation(x_qt[h][:], q_ps[:], ACT.Copy).then_inc(qt_copied, 1)

                def normalise(n, b, h):
                    act.wait_ge(offset_ready, n + 1)
                    act.wait_ge(stored[h], 16 * b + 16)
                    for t in range(HT):
                        last = nc.scalar.activation(result[h][:, t, :], y2[h][:, t, :], ACT.Identity,
                                                    scale=rstd[1][:, t:t + 1], bias=offset[:, t:t + 1])
                    last.then_inc(result_ready, 1)
                    act.wait_ge(result_ready, n + 1)
                    dst = A["result"][bass.ds(b * N + h * HALF, HALF), :]
                    act.dma_start(dst.rearrange("(t p) d -> p t d", p=P), result[h][:]).then_inc(stored[h], 16)

                run(act, [(1, scale_input), (0, copy_rounded), (3, copy_output), (-1, normalise)])
                for h in two:
                    act.wait_ge(stored[h], 16 * nb + 16)

            @block.vector
            def _(dve):
                def row_stats(y, i, n):
                    for t in range(HT):
                        last = nc.vector.bn_stats(stats[i][:, t, :], y[:, t, :])
                    last.then_inc(stats_ready[i], 1)
                    wait_apart(dve, passed, stats_ready[i], n + 1)
                    for t in range(HT):
                        last = nc.vector.bn_aggr(mean_var[i][:, t, :], stats[i][:, t, :])
                    last.then_inc(mv_ready[i], 1)

                def first_stats(n, b, h):
                    dve.wait_ge(y1_ready, n + 1)
                    row_stats(y1[h], 0, n)

                def second_stats(n, b, h):
                    wait_past(dve, offset_ready, n)
                    dve.wait_ge(y2_ready, n + 1)
                    row_stats(y2[h], 1, n)

                def add_attention(n, b, h):
                    dve.wait_ge(proj_ready, n + 1)
                    wait_past(dve, x1_ready, n)
                    nc.vector.tensor_tensor(y1[h][:], proj_ps[:], x_in[h][:], ALU.add).then_inc(y1_ready, 1)

                def normalise(n, b, h):
                    dve.wait_ge(rstd_ready[0], n + 1)
                    wait_past(dve, scaled_ready, n - 1)
                    wait_past(dve, y2_ready, n - 1)
                    for t in range(HT):
                        last = nc.vector.tensor_scalar(x1[h][:, t, :], y1[h][:, t, :], mean_var[0][:, t, 0:1],
                                                       rstd[0][:, t:t + 1], ALU.subtract, ALU.mult)
                    last.then_inc(x1_ready, 1)

                def find_magic(n, b, h):
                    dve.wait_ge(scaled_ready, n + 1)
                    wait_past(dve, xq_ready, n - 1)
                    nc.vector.tensor_scalar(clipped[h][:], scaled[h][:], FP8_MAX, -FP8_MAX, ALU.min, ALU.max
                                            ).then_inc(clipped_ready, 1)
                    dve.wait_ge(clipped_ready, n + 1)
                    nc.vector.tensor_scalar(power[:].bitcast(U32), clipped[h][:].bitcast(U32), 0x7F800000, None,
                                            ALU.bitwise_and).then_inc(power_ready, 1)
                    dve.wait_ge(power_ready, n + 1)
                    nc.vector.tensor_scalar(magic[h][:], power[:], ROUND_TO_4_BITS, FP8_MIN_NORMAL * ROUND_TO_4_BITS,
                                            ALU.mult, ALU.max).then_inc(magic_ready, 1)

                def add_linear(n, b, h):
                    dve.wait_ge(ffn_ready, n + 1)
                    dve.wait_ge(stored[h], 16 * b + 16)
                    nc.vector.tensor_tensor(y2[h][:], ffn_ps[:], x1[h][:], ALU.add).then_inc(y2_ready, 1)

                for h in two:
                    dve.sem_inc(stored[h], 16)
                run(dve, [(-1, add_linear), (1, normalise), (-1, second_stats), (1, find_magic),
                          (2, add_attention), (2, first_stats)])

            @block.gpsimd
            def _(pool):
                def deviation(i, n):
                    pool.wait_ge(mv_ready[i], n + 1)
                    nc.gpsimd.tensor_tensor(var_eps[i][:], mean_var[i][:, :, 1], W["eps"][:], ALU.add
                                            ).then_inc(eps_added[i], 1)
                    pool.wait_ge(eps_added[i], n + 1)
                    nc.gpsimd.tensor_tensor(rstd[i][:], var_eps[i][:], W["minus_half"][:], ALU.pow
                                            ).then_inc(rstd_ready[i], 1)

                def first_norm(n, b, h):
                    deviation(0, n)

                def add_magic(n, b, h):
                    pool.wait_ge(magic_ready, n + 1)
                    wait_past(pool, xq_ready, n)
                    nc.gpsimd.tensor_tensor(shifted[:], clipped[h][:], magic[h][:], ALU.add).then_inc(shifted_ready, 1)

                def take_magic(n, b, h):
                    pool.wait_ge(shifted_ready, n + 1)
                    wait_past(pool, qt_ready, n - 1)
                    nc.gpsimd.tensor_tensor(x_q[h][:], shifted[:], magic[h][:], ALU.subtract).then_inc(xq_ready, 1)

                def second_norm(n, b, h):
                    wait_past(pool, result_ready, n)
                    deviation(1, n)
                    nc.gpsimd.tensor_tensor(neg_mean[:], mean_var[1][:, :, 0], W["minus_one"][:], ALU.mult
                                            ).then_inc(rstd_ready[1], 1)
                    pool.wait_ge(rstd_ready[1], 2 * (n + 1))
                    nc.gpsimd.tensor_tensor(offset[:], neg_mean[:], rstd[1][:], ALU.mult).then_inc(offset_ready, 1)

                run(pool, [(1, first_norm), (0, take_magic), (-1, second_norm), (1, add_magic)])


def layer_program(nc, x, W_qkv, u_qkv, sigma_qkv, W_proj, u_proj, sigma_proj, weight, bias, input_scale,
                  weight_scale, result, nb=NB):
    A = {"x": x.rearrange("b n d -> (b n) d"), "W_qkv": W_qkv, "u_qkv": u_qkv, "sigma_qkv": sigma_qkv,
         "W_proj": W_proj, "u_proj": u_proj, "sigma_proj": sigma_proj, "weight": weight, "bias": bias,
         "input_scale": input_scale, "weight_scale": weight_scale,
         "result": result.rearrange("b n d -> (b n) d")}
    S = {
        "qk": nc.dram_tensor("scratch_qk", [nb, NG, 3, P, N], BF16, kind="Internal").ap(),
        "v": nc.dram_tensor("scratch_v", [nb, NG, P, NT * GD], FP32, kind="Internal").ap(),
        "out": nc.dram_tensor("scratch_out", [nb, 2, P, HT, D], FP32, kind="Internal").ap(),
    }
    with ExitStack() as ctx:
        m = Memory(nc, ctx)
        W = {
            "qk": m.sb("w_qk", [P, KC, NG, P]),
            "v": m.sb("w_v", [P, KC, D]),
            "proj": m.sb("w_proj", [P, KC, D]),
            "ffn": m.sb("w_ffn", [P, 3, KC, D], BF16),
            "bias3": m.sb("w_bias3", [P, D], BF16),
            "ones_b": m.sb("w_ones_b", [P, P], BF16),
            "ident": m.sb("w_ident", [P, P]),
            "ident_b": m.sb("w_ident_b", [P, P], BF16),
            "causal": m.sb("w_causal", [P, P], BF16),
            "minus_half": m.sb("w_minus_half", [P, HT]),
            "minus_one": m.sb("w_minus_one", [P, HT]),
            "eps": m.sb("w_eps", [P, HT]),
            "inv_input_scale": m.sb("w_inv_input_scale", [P, 1]),
        }
        weights_block(nc, m, W, A)
        with ExitStack() as attend_ctx:
            t = Memory(nc, attend_ctx)
            T = {
                "q_stack": [t.sb(f"a_q{i}", [P, HG, N], BF16) for i in range(NG)],
                "k_stack": [t.sb(f"a_k{i}", [P, HG, N], BF16) for i in range(NG)],
                "v_in": [t.sb(f"a_vin{i}", [P, NT, GD]) for i in range(2)],
                "stack_loaded": [t.sem(f"a_stack_loaded{i}") for i in range(NG)],
                "v_loaded": [t.sem(f"a_v_loaded{i}") for i in range(2)],
            }
            project_block(nc, W, A, S, T, nb)
            attend_block(nc, W, S, T, nb)
        finish_block(nc, W, A, S, nb)


INPUTS = ["L0_attn_batch", "L0_attn_W_qkv", "L0_attn_u_qkv", "L0_attn_sigma_qkv", "L0_attn_W_proj",
          "L0_attn_u_proj", "L0_attn_sigma_proj", "L0_ffn_weight_fp8", "L0_ffn_bias", "L0_ffn_input_scale",
          "L0_ffn_weight_scale"]


def kernel(**inputs):
    import numpy as np
    import concourse.bacc as bacc
    from concourse.bass_utils import run_bass_kernel_spmd

    nc = bacc.Bacc("TRN2", target_bir_lowering=False, num_devices=1)
    arrays, args = {}, []
    for name in INPUTS:
        a = np.ascontiguousarray(inputs[name])
        arrays[name] = a
        args.append(nc.dram_tensor(name, a.shape, mybir.dt.from_np(a.dtype), kind="ExternalInput").ap())
    args.append(nc.dram_tensor("result", [NB, N, D], FP32, kind="ExternalOutput").ap())
    layer_program(nc, *args)
    r = run_bass_kernel_spmd(nc, [arrays], core_ids=[0])
    return r.results[0]["result"]
```
